# Optimizing a Trainium2 kernel written in Bass

```python
import numpy as np
import jax
import jax.numpy as jnp

def _softmax(x, axis=-1):
    return jax.nn.softmax(x, axis=axis)

def _gelu(x):
    return jax.nn.gelu(x, approximate=True)

def _silu(x):
    return jax.nn.silu(x)

def _sigmoid(x):
    return jax.nn.sigmoid(x)

def _layernorm(x, axis=-1, eps=1e-05):
    m = jnp.mean(x, axis=axis, keepdims=True)
    v = jnp.var(x, axis=axis, keepdims=True)
    return (x - m) / jnp.sqrt(v + eps)

def _scatter_add(tgt, idx, src, axis=0):
    return tgt.at[idx].add(src)

def _segment_sum(src, seg, n):
    return jax.ops.segment_sum(src, seg, n)
kernel_name = 'mk_adj_preln_d2_adj_r2_9cf906'

def setup_inputs(seed: int=0):
    np.random.seed(seed)
    _w = jnp.asarray

    def _rec_inputs():
        import jax
        import jax.numpy as jnp
        _gk = jax.random.key(seed)
        x = -0.000125 + 0.9999 * jax.random.normal(jax.random.fold_in(_gk, 1), (16, 512, 256), jnp.float32)
        _w = (1.0 + jnp.arange(512, dtype=jnp.float32)) ** (-0.5)
        _w = _w / _w.mean()
        _pij = jnp.clip(0.03125 * _w[:, None] * _w[None, :], 0.0, 1.0)
        _a = jax.random.uniform(jax.random.fold_in(_gk, 2), (512, 512)) < _pij
        _af = _a.astype(jnp.float32)
        adj = _af
        return (x, adj)
    x, adj = _rec_inputs()

    def _L0_gnn_setup():
        import jax, jax.numpy as jnp
        import numpy as np
        ALPHA = 0.2
        key = jax.random.key(seed)
        k0, k1, k2, k3 = jax.random.split(key, 4)
        B, N, C, F = (64, 512, 256, 256)
        x = jax.random.normal(k0, (B, N, C), dtype=jnp.float32)
        W = jax.random.normal(k1, (C, F), dtype=jnp.float32) * (1.414 / np.sqrt(C + F))
        a = jax.random.normal(k2, (2 * F, 1), dtype=jnp.float32) * (1.414 / np.sqrt(2 * F + 1))
        beta = jnp.ones((1,), dtype=jnp.float32)
        mask = (jax.random.uniform(k3, (N, N)) < 0.3).astype(jnp.float32)
        return {'x': x, 'W': W, 'a': a, 'beta': beta, 'mask': mask}
    _L0_gnn_all = _L0_gnn_setup()
    _L0_gnn_in = {k: v for k, v in _L0_gnn_all.items() if k in ('W', 'a', 'beta')}
    del _L0_gnn_all

    def _L1_gnn_setup():
        import jax, jax.numpy as jnp
        import numpy as np
        B, N, D = (8, 1024, 256)
        key = jax.random.key(seed)
        k1, k2, k3, k4, k5 = jax.random.split(key, 5)
        neuron_states = jax.random.normal(k1, (B, N, D), dtype=jnp.float32)
        adjacency = jax.random.randint(k2, (N, N), 0, 2).astype(jnp.float32)
        scale = 1.0 / np.sqrt(D)
        Wq = jax.random.normal(k3, (D, D), dtype=jnp.float32) * scale
        Wk = jax.random.normal(k4, (D, D), dtype=jnp.float32) * scale
        Wv = jax.random.normal(k5, (D, D), dtype=jnp.float32) * scale
        return {'neuron_states': neuron_states, 'adjacency': adjacency, 'Wq': Wq, 'Wk': Wk, 'Wv': Wv}
    _L1_gnn_all = _L1_gnn_setup()
    _L1_gnn_in = {k: v for k, v in _L1_gnn_all.items() if k in ('Wq', 'Wk', 'Wv')}
    del _L1_gnn_all
    return {'x': x, 'adj': adj, 'L0_gnn_W': _L0_gnn_in['W'], 'L0_gnn_a': _L0_gnn_in['a'], 'L0_gnn_beta': _L0_gnn_in['beta'], 'L1_gnn_Wq': _L1_gnn_in['Wq'], 'L1_gnn_Wk': _L1_gnn_in['Wk'], 'L1_gnn_Wv': _L1_gnn_in['Wv']}

def reference(x, adj, L0_gnn_W, L0_gnn_a, L0_gnn_beta, L1_gnn_Wq, L1_gnn_Wk, L1_gnn_Wv):
    import jax
    import jax.numpy as jnp

    def _L0_gnn_ref(x, W, a, beta, mask):
        import jax, jax.numpy as jnp
        import numpy as np
        ALPHA = 0.2
        F_ = W.shape[1]
        h = jnp.einsum('bnc,cf->bnf', x, W)
        a1, a2 = (a[:F_, 0], a[F_:, 0])
        s1 = jnp.einsum('bnf,f->bn', h, a1)
        s2 = jnp.einsum('bnf,f->bn', h, a2)
        e = jax.nn.leaky_relu(s1[:, :, None] + s2[:, None, :], negative_slope=ALPHA)
        e = e * mask[None, :, :]
        att = jax.nn.softmax(e, axis=2)
        h_prime = jnp.einsum('bij,bjf->bif', att, h)
        return jax.nn.elu(h_prime + beta * h)

    def _L1_gnn_ref(neuron_states, adjacency, Wq, Wk, Wv):
        import jax, jax.numpy as jnp
        import numpy as np
        B, N, D = (8, 1024, 256)
        q = jnp.einsum('bnd,ed->bne', neuron_states, Wq)
        k = jnp.einsum('bnd,ed->bne', neuron_states, Wk)
        v = jnp.einsum('bnd,ed->bne', neuron_states, Wv)
        rel = jnp.einsum('bnd,bmd->bnm', q, k)
        rel = adjacency.T[None, :, :] * rel
        rel = rel / jnp.linalg.norm(rel, axis=2, keepdims=True)
        return jnp.einsum('bnm,bmd->bnd', rel, v)
    h = jnp.maximum(_layernorm(x, axis=-1), 0.0)
    x = x + _L0_gnn_ref(h, L0_gnn_W, L0_gnn_a, L0_gnn_beta, adj)
    h = jnp.maximum(_layernorm(x, axis=-1), 0.0)
    x = x + _L1_gnn_ref(h, adj, L1_gnn_Wq, L1_gnn_Wk, L1_gnn_Wv)
    return x

_drawn_inputs = setup_inputs


def setup_inputs(seed=0):
    import zlib

    import numpy as np

    out = dict(_drawn_inputs(seed))
    spreads = {}
    factors = {'L0_gnn_a': 6.591}
    for name, (base, spread) in spreads.items():
        noise = np.random.default_rng([zlib.crc32(name.encode()), seed]).standard_normal(out[name].shape)
        drawn = base * np.exp(spread * noise) if base else spread * noise
        out[name] = jnp.asarray(drawn.astype(out[name].dtype))
    for name, factor in factors.items():
        out[name] = (out[name] * factor).astype(out[name].dtype)
    return out
```

```python
from contextlib import ExitStack

import concourse.bass as bass
from concourse import mybir

F32 = mybir.dt.float32
F32R = mybir.dt.float32r
ALU = mybir.AluOpType
ACT = mybir.ActivationFunctionType

P = 128
LEAK = 0.2
EPS = 1e-5
LOWEST = -3.4028235e38
DMA = 16


class Graph:

    def __init__(self, now, before, index=None, dma_now=None, dma_before=None):
        self.now, self.before, self.index = now, before, index
        self.dma_now, self.dma_before = dma_now, dma_before


def graph(b):
    return Graph(b + 1, b, b, DMA * (b + 1), DMA * b)


def wait(eng, sem, count):
    if not (isinstance(count, int) and count <= 0):
        eng.wait_ge(sem, count)


def run_steps(eng, B, step):
    step(graph(0), None, graph(1))
    step(graph(1), graph(0), graph(2))
    with eng.Fori(2, B - 1) as i:
        n2, n1, n0 = eng.snap(i + 2), eng.snap(i + 1), eng.snap(i - 1)
        d2, d1, d0, dm = eng.snap(n2 * DMA), eng.snap(n1 * DMA), eng.snap(i * DMA), eng.snap(n0 * DMA)
        for count in (n2, n1, n0, d2, d1, d0, dm):
            eng.compute_val(count)
        step(Graph(n1, i, i, d1, d0), Graph(i, n0, n0, d0, dm), Graph(n2, n1, n1, d2, d1))
    step(graph(B - 1), graph(B - 2), None)
    step(None, graph(B - 1), None)


def build(nc, x, adj, W, a, beta, Wq, Wk, Wv, out):
    B, N, C = x.shape
    NT, CT = N // P, C // P
    assert N == 512 and C == 256 and W.shape == (C, C)

    with ExitStack() as ctx:
        def sb(name, shape, dt=F32):
            return ctx.enter_context(nc.sbuf_tensor(name, [P, *shape], dt))

        def sem(name):
            return ctx.enter_context(nc.semaphore(name))

        def sems(name, n):
            return [sem(f"{name}_{t}") for t in range(n)]

        def pair(name, shape):
            return sb(name + "_hi", shape, F32R), sb(name + "_lo", shape, F32R)

        ident = sb("ident", [P])
        ones = sb("ones", [P])
        adj_sb = sb("adj_sb", [NT, N])
        minus_half = sb("minus_half", [NT])
        beta_sb = sb("beta_sb", [1])
        beta_ident = sb("beta_ident", [P])
        wa1_rows = sb("wa1_rows", [C])
        W_hi, W_lo = pair("W", [CT, C])
        G_hi, G_lo = pair("G", [CT, C])
        WvT_hi, WvT_lo = pair("WvT", [CT, C])
        wa2_hi, wa2_lo = pair("wa2", [CT, P])

        x_sb = sb("x_sb", [NT, C])
        x_res = sb("x_res", [NT, C])
        bn0 = sb("bn0", [NT, 6])
        mom0 = sb("mom0", [NT, 2])
        rstd0 = sb("rstd0", [NT])
        bias0 = sb("bias0", [NT])
        small0 = sb("small0", [2, NT])
        h0 = sb("h0", [NT, C])
        h0_hi, h0_lo = pair("h0", [NT, C])
        h0T_hi, h0T_lo = pair("h0T", [CT, N])
        s1 = sb("s1", [NT])
        s1_products = sb("s1_products", [C])
        z = sb("z", [NT, N])
        e = sb("e", [NT, N])
        att = sb("att", [NT, N])
        row_max = sb("row_max", [NT])
        minus_max = sb("minus_max", [NT])
        row_sum = sb("row_sum", [NT])
        row_inv = sb("row_inv", [NT])
        attT_hi, attT_lo = pair("attT", [NT, N])
        mixT_hi, mixT_lo = pair("mixT", [CT, N])
        exp_y = sb("exp_y", [NT, C])
        elu_x = sb("elu_x", [NT, C])
        x1p = sb("x1p", [NT, C])

        x1 = sb("x1", [NT, C])
        bn1 = sb("bn1", [NT, 6])
        mom1 = sb("mom1", [NT, 2])
        rstd1 = sb("rstd1", [NT])
        bias1 = sb("bias1", [NT])
        small1 = sb("small1", [2, NT])
        g = sb("g", [NT, C])
        g_hi, g_lo = pair("g", [NT, C])
        gT_hi, gT_lo = pair("gT", [CT, N])
        tT_hi, tT_lo = pair("tT", [CT, N])
        rel = sb("rel", [NT, N])
        rel_hi, rel_lo = pair("rel", [NT, N])
        squares = sb("squares", [NT, N])
        sum_sq = sb("sum_sq", [N])
        aggT_hi, aggT_lo = pair("aggT", [CT, N])
        norm_sq = sb("norm_sq", [NT])
        inv_norm = sb("inv_norm", [NT])
        y_out = sb("y_out", [NT, C])

        W_in, Wq_in, Wk_in, Wv_in = (z[:, t, :].rearrange("p (t c) -> p t c", t=CT) for t in range(4))
        WT, a_rep = (e[:, t, :].rearrange("p (t c) -> p t c", c=c) for t, c in ((0, C), (1, P)))
        a_col = e[:, 2, 0:2 * CT]
        beta_row = e[0:1, 3, 0:1]

        ps_A, ps_B, ps_C, ps_D = (ctx.enter_context(nc.psum_tensor(f"ps_{n}", [P, 2, N], F32)) for n in "ABCD")
        norm_ps = ps_A[:, 0, 0:NT]
        rel_ps = [ps_A[:, 0, :], ps_A[:, 1, :], ps_B[:, 0, :], ps_B[:, 1, :]]
        attT_ps = [ps_C[:, 0, :], ps_C[:, 1, :], ps_D[:, 1, :], ps_D[:, 0, :]]

        def rows(pair_of_banks, t):
            return pair_of_banks[:, t // 2, (t % 2) * C:(t % 2 + 1) * C]

        weights_in = sem("weights_in")
        adj_in = sem("adj_in")
        zeroed = sem("zeroed")
        consts_made = sem("consts_made")
        a_spread = sem("a_spread")
        turned = sem("turned")
        turned_copied = sem("turned_copied")
        made = sem("made")
        setup_chain = sem("setup_chain")
        setup_done = sem("setup_done")

        x_in, xres_in = sem("x_in"), sem("xres_in")
        bn0_done, mom0_done = sem("bn0_done"), sem("mom0_done")
        var0_done, rstd0_done, bias0_done = sem("var0_done"), sem("rstd0_done"), sem("bias0_done")
        h0_done = sems("h0_done", NT)
        h0_hi_done, h0_lo_done = sem("h0_hi_done"), sem("h0_lo_done")
        h0_turned = sems("h0_turned", CT)
        h0T_hi_done, h0T_lo_done = sems("h0T_hi_done", CT), sems("h0T_lo_done", CT)
        s1_done = sems("s1_done", NT)
        s2_done = sem("s2_done")
        z_done, leaky_done = sems("z_done", NT), sems("leaky_done", NT)
        e_done, max_done = sems("e_done", NT), sems("max_done", NT)
        exp_done, inv_done = sems("exp_done", NT), sems("inv_done", NT)
        scaled, att_done = sems("scaled", NT), sems("att_done", NT)
        att_turned = sems("att_turned", NT)
        attT_hi_done, attT_lo_done = sems("attT_hi_done", NT), sem("attT_lo_done")
        mix_done = sems("mix_done", CT)
        mixT_hi_done, mixT_lo_done = sems("mixT_hi_done", CT), sems("mixT_lo_done", CT)
        y_done, exp_y_done = sems("y_done", 2), sems("exp_y_done", 2)
        elu_x_done, x1p_done = sems("elu_x_done", 2), sems("x1p_done", 2)

        x1_done = sem("x1_done")
        bn1_done, mom1_done = sem("bn1_done"), sem("mom1_done")
        var1_done, rstd1_done, bias1_done = sem("var1_done"), sem("rstd1_done"), sem("bias1_done")
        g_done = sems("g_done", NT)
        g_hi_done, g_lo_done = sem("g_hi_done"), sem("g_lo_done")
        g_turned = sems("g_turned", CT)
        gT_hi_done, gT_lo_done = sems("gT_hi_done", CT), sems("gT_lo_done", CT)
        t_done = sems("t_done", CT)
        tT_hi_done, tT_lo_done = sems("tT_hi_done", CT), sems("tT_lo_done", CT)
        rel_mm_done, rel_done = sems("rel_mm_done", NT), sems("rel_done", NT)
        rel_hi_done, rel_lo_done = sems("rel_hi_done", NT), sems("rel_lo_done", NT)
        squared, sum_sq_done = sems("squared", NT), sems("sum_sq_done", NT - 1)
        agg_done = sems("agg_done", CT)
        aggT_hi_done, aggT_lo_done = sems("aggT_hi_done", CT), sems("aggT_lo_done", CT)
        norm_mm_done, norm_copied, inv_norm_done = sem("norm_mm_done"), sem("norm_copied"), sem("inv_norm_done")
        out_done = sems("out_done", 2)
        out_added = sems("out_added", 2)
        stored = sem("stored")

        def tiled(w):
            return w.rearrange("(t p) c -> p t c", p=P)

        block = ctx.enter_context(nc.Block())

        @block.sync
        def _(sp):
            sp.dma_start(x_sb[:], tiled(x[0])).then_inc(x_in, DMA)
            for dst, src in ((W_in, W), (Wq_in, Wq), (Wk_in, Wk), (Wv_in, Wv)):
                sp.dma_start(dst, tiled(src)).then_inc(weights_in, DMA)
            with nc.allow_non_contiguous_dma(reason="the 512 numbers of a, once"):
                sp.dma_start(a_col, a.rearrange("(t p) o -> p (t o)", p=P)).then_inc(weights_in, DMA)
            sp.dma_start(beta_row, beta.rearrange("(o n) -> o n", o=1)).then_inc(weights_in, DMA)
            sp.dma_start(adj_sb[:], tiled(adj)).then_inc(adj_in, DMA)
            sp.dma_start(x_res[:], tiled(x[0])).then_inc(xres_in, DMA)

            def step(L0, L1, nxt):
                if nxt:
                    wait(sp, h0_done[NT - 1], nxt.before)
                    sp.dma_start(x_sb[:], tiled(x[nxt.index])).then_inc(x_in, DMA)
                    wait(sp, elu_x_done[1], nxt.before)
                    sp.dma_start(x_res[:], tiled(x[nxt.index])).then_inc(xres_in, DMA)
                if L1:
                    wait(sp, out_added[1], L1.now)
                    sp.dma_start(tiled(out[L1.index]), y_out[:]).then_inc(stored, DMA)

            run_steps(sp, B, step)
            sp.wait_ge(stored, DMA * B)

        @block.gpsimd
        def _(pool):
            pool.memset(ident[:], 0.0).then_inc(zeroed, 1)
            pool.memset(ones[:], 1.0).then_inc(consts_made, 1)
            pool.memset(minus_half[:], -0.5).then_inc(consts_made, 1)
            pool.wait_ge(zeroed, 1)
            pool.affine_select(out=ident[:], in_=ident[:], compare_op=ALU.not_equal, fill=1.0, base=0,
                               pattern=[[-1, P]], channel_multiplier=1).then_inc(consts_made, 1)
            pool.wait_ge(consts_made, 3)

            def moments(mom, small, rstd, bias, mom_done, var_done, rstd_done, bias_done, h_done, b):
                pool.wait_ge(consts_made, 3)
                wait(pool, h_done[NT - 1], b.before)
                wait(pool, mom_done, b.now)
                pool.tensor_scalar(small[:, 0, :], mom[:, :, 1], 1.0, EPS, ALU.mult, ALU.add)
                pool.tensor_scalar(small[:, 1, :], mom[:, :, 0], -1.0, 0.0, ALU.mult, ALU.add).then_inc(var_done, 1)
                wait(pool, var_done, b.now)
                pool.tensor_tensor(rstd[:], small[:, 0, :], minus_half[:], ALU.pow).then_inc(rstd_done, 1)
                wait(pool, rstd_done, b.now)
                pool.tensor_tensor(bias[:], small[:, 1, :], rstd[:], ALU.mult).then_inc(bias_done, 1)

            def h0_low(b):
                wait(pool, mix_done[CT - 1], b.before)
                wait(pool, h0_hi_done, b.now)
                pool.tensor_tensor(h0_lo[:], h0[:], h0_hi[:].bitcast(F32), ALU.subtract).then_inc(h0_lo_done, 1)

            def step(L0, L1, nxt):
                if L0:
                    for t in range(NT):
                        wait(pool, scaled[t], L0.now)
                        d = att[:, t, t * P:(t + 1) * P]
                        pool.tensor_tensor(d, d, beta_ident[:], ALU.add).then_inc(att_done[t], 1)
                        if L1:
                            rel_low(t, L1)
                elif L1:
                    for t in range(NT):
                        rel_low(t, L1)
                if nxt:
                    moments(mom0, small0, rstd0, bias0, mom0_done, var0_done, rstd0_done, bias0_done, h0_done, nxt)
                if L1:
                    wait(pool, norm_mm_done, L1.before)
                    for t in range(1, NT):
                        wait(pool, squared[t], L1.now)
                        if t > 1:
                            wait(pool, sum_sq_done[t - 2], L1.now)
                        pool.tensor_tensor(sum_sq[:], squares[:, 0, :] if t == 1 else sum_sq[:], squares[:, t, :],
                                           ALU.add).then_inc(sum_sq_done[t - 1], 1)
                if L0:
                    moments(mom1, small1, rstd1, bias1, mom1_done, var1_done, rstd1_done, bias1_done, g_done, L0)
                if L1:
                    wait(pool, norm_copied, L1.now)
                    pool.tensor_tensor(inv_norm[:], norm_sq[:], minus_half[:], ALU.pow).then_inc(inv_norm_done, 1)
                if nxt:
                    h0_low(nxt)
                if L0:
                    pool.wait_ge(consts_made, 3)
                    wait(pool, out_added[1], L0.before)
                    wait(pool, x1p_done[1], L0.now)
                    pool.tensor_scalar(x1[:], x1p[:], 1.0, -1.0, ALU.mult, ALU.add).then_inc(x1_done, 1)
                    wait(pool, agg_done[CT - 1], L0.before)
                    wait(pool, g_hi_done, L0.now)
                    pool.tensor_tensor(g_lo[:], g[:], g_hi[:].bitcast(F32), ALU.subtract).then_inc(g_lo_done, 1)

            def rel_low(t, b):
                wait(pool, agg_done[CT - 1], b.before)
                wait(pool, rel_hi_done[t], b.now)
                pool.tensor_tensor(rel_lo[:, t, :], rel[:, t, :], rel_hi[:, t, :].bitcast(F32),
                                   ALU.subtract).then_inc(rel_lo_done[t], 1)

            moments(mom0, small0, rstd0, bias0, mom0_done, var0_done, rstd0_done, bias0_done, h0_done, graph(0))
            h0_low(graph(0))
            pool.wait_ge(setup_done, 1)
            run_steps(pool, B, step)

        @block.scalar
        def _(act):
            def upper(dst, src, ready, done, b, reader=None):
                if reader:
                    wait(act, reader, b.before)
                wait(act, ready, b.now)
                act.activation(dst, src, ACT.Copy).then_inc(done, 1)

            def normalise(dst, src, rstd, bias, bias_done, done, b):
                wait(act, bias_done, b.now)
                for t in range(NT):
                    act.activation(dst[:, t, :], src[:, t, :], ACT.Relu, bias=bias[:, t:t + 1],
                                   scale=rstd[:, t:t + 1]).then_inc(done[t], 1)

            def normalise0(b):
                wait(act, h0_turned[CT - 1], b.before)
                wait(act, s1_done[NT - 1], b.before)
                wait(act, h0_lo_done, b.before)
                normalise(h0, x_sb, rstd0, bias0, bias0_done, h0_done, b)

            def scores(t, b):
                wait(act, leaky_done[t], b.before)
                wait(act, s1_done[t], b.now)
                wait(act, s2_done, b.now)
                act.activation(z[:, t, :], ps_D[:, 0, :], ACT.Identity, bias=s1[:, t:t + 1]).then_inc(z_done[t], 1)

            def exponent(t, b):
                wait(act, att_turned[t], b.before)
                wait(act, inv_done[t], b.before)
                wait(act, max_done[t], b.now)
                act.activation(att[:, t, :], e[:, t, :], ACT.Exp, bias=minus_max[:, t:t + 1],
                               accum_out=row_sum[:, t:t + 1]).then_inc(exp_done[t], 1)

            def rel_parts(t, b):
                wait(act, agg_done[CT - 1], b.before)
                wait(act, rel_done[t], b.now)
                act.activation(rel_hi[:, t, :], rel[:, t, :], ACT.Copy).then_inc(rel_hi_done[t], 1)
                wait(act, sum_sq_done[NT - 2], b.before)
                act.activation(squares[:, t, :], rel[:, t, :], ACT.Square).then_inc(squared[t], 1)

            def step(L0, L1, nxt):
                if L1:
                    for c in range(CT):
                        upper(gT_hi[:, c, :], ps_A[:, c, :], g_turned[c], gT_hi_done[c], L1, rel_mm_done[NT - 1])
                if L0:
                    for c in range(CT):
                        upper(h0T_hi[:, c, :], ps_B[:, c, :], h0_turned[c], h0T_hi_done[c], L0, s2_done)
                if L1:
                    for c in range(CT):
                        upper(tT_hi[:, c, :], ps_C[:, c, :], t_done[c], tT_hi_done[c], L1, rel_mm_done[NT - 1])
                if L0:
                    scores(0, L0)
                    scores(1, L0)
                for t in range(NT):
                    if L0:
                        exponent(t, L0)
                        if t + 2 < NT:
                            scores(t + 2, L0)
                    if L1:
                        rel_parts(t, L1)
                if L0:
                    for t in range(NT):
                        upper(attT_hi[:, :, t * P:(t + 1) * P], attT_ps[t].rearrange("p (j n) -> p j n", j=NT),
                              att_turned[t], attT_hi_done[t], L0, mix_done[CT - 1])
                if nxt:
                    normalise0(nxt)
                if L0:
                    for c in range(CT):
                        upper(mixT_hi[:, c, :], ps_A[:, c, :], mix_done[c], mixT_hi_done[c], L0, y_done[1])
                if L1:
                    upper(aggT_hi[:, 0, :], ps_B[:, 0, :], agg_done[0], aggT_hi_done[0], L1, out_done[1])
                if L0:
                    for c in range(2):
                        wait(act, elu_x_done[c], L0.before)
                        wait(act, y_done[c], L0.now)
                        act.activation(exp_y[:, 2 * c:2 * c + 2, :], ps_C[:, c, :].rearrange("p (t c) -> p t c", t=2),
                                       ACT.Exp).then_inc(exp_y_done[c], 1)
                if L1:
                    upper(aggT_hi[:, 1, :], ps_B[:, 1, :], agg_done[1], aggT_hi_done[1], L1)
                if L0:
                    wait(act, g_turned[CT - 1], L0.before)
                    wait(act, g_lo_done, L0.before)
                    normalise(g, x1p, rstd1, bias1, bias1_done, g_done, L0)

            normalise0(graph(0))
            run_steps(act, B, step)

        @block.vector
        def _(dve):
            def lower(dst, src, hi, hi_done, done, b, reader=None):
                if reader:
                    wait(dve, reader, b.before)
                wait(dve, hi_done, b.now)
                ins = dve.tensor_tensor(dst, src, hi.bitcast(F32), ALU.subtract)
                if done:
                    ins.then_inc(done, 1)

            def statistics(src, bn, mom, bn_done, mom_done, rstd_done, b):
                for t in range(NT):
                    ins = dve.bn_stats(bn[:, t, :], src[:, t, :])
                ins.then_inc(bn_done, 1)
                dve.wait_ge(x_in, DMA)
                wait(dve, rstd_done, b.before)
                wait(dve, bn_done, b.now)
                for t in range(NT):
                    ins = dve.bn_aggr(mom[:, t, :], bn[:, t, :])
                ins.then_inc(mom_done, 1)

            def statistics0(b):
                wait(dve, mom0_done, b.before)
                wait(dve, x_in, b.dma_now)
                statistics(x_sb, bn0, mom0, bn0_done, mom0_done, rstd0_done, b)

            def upper_h0(b):
                wait(dve, mix_done[CT - 1], b.before)
                wait(dve, h0_lo_done, b.before)
                wait(dve, h0_done[NT - 1], b.now)
                dve.tensor_copy(h0_hi[:], h0[:]).then_inc(h0_hi_done, 1)

            def score1(b):
                for t in range(NT):
                    wait(dve, z_done[t], b.before)
                    wait(dve, h0_done[t], b.now)
                    if t:
                        wait(dve, s1_done[t - 1], b.now)
                    else:
                        wait(dve, s1_done[NT - 1], b.before)
                    dve.wait_ge(adj_in, DMA)
                    dve.tensor_tensor_reduce(s1_products[:], h0[:, t, :], wa1_rows[:], 1.0, 0.0, ALU.mult, ALU.add,
                                             s1[:, t:t + 1]).then_inc(s1_done[t], 1)

            def masked_max(t, b):
                wait(dve, exp_done[t], b.before)
                wait(dve, z_done[t], b.now)
                dve.scalar_tensor_tensor(out=e[:, t, :], in0=z[:, t, :], scalar=LEAK, in1=z[:, t, :], op0=ALU.mult,
                                         op1=ALU.max).then_inc(leaky_done[t], 1)
                dve.wait_ge(adj_in, DMA)
                wait(dve, leaky_done[t], b.now)
                dve.tensor_tensor_reduce(e[:, t, :], e[:, t, :], adj_sb[:, t, :], 1.0, LOWEST, ALU.mult, ALU.max,
                                         row_max[:, t:t + 1]).then_inc(e_done[t], 1)
                wait(dve, e_done[t], b.now)
                dve.tensor_scalar(minus_max[:, t:t + 1], row_max[:, t:t + 1], -1.0, None,
                                  ALU.mult).then_inc(max_done[t], 1)

            def softmax_scale(t, b):
                wait(dve, exp_done[t], b.now)
                dve.reciprocal(row_inv[:, t:t + 1], row_sum[:, t:t + 1]).then_inc(inv_done[t], 1)
                wait(dve, inv_done[t], b.now)
                dve.tensor_scalar(att[:, t, :], att[:, t, :], row_inv[:, t:t + 1], None,
                                  ALU.mult).then_inc(scaled[t], 1)

            def rel_mask(t, b):
                wait(dve, rel_lo_done[t], b.before)
                wait(dve, squared[t], b.before)
                wait(dve, rel_mm_done[t], b.now)
                dve.tensor_tensor(rel[:, t, :], rel_ps[t], adj_sb[:, t, :], ALU.mult).then_inc(rel_done[t], 1)

            def step(L0, L1, nxt):
                if L1:
                    for c in range(CT):
                        lower(gT_lo[:, c, :], ps_A[:, c, :], gT_hi[:, c, :], gT_hi_done[c], gT_lo_done[c], L1,
                              rel_mm_done[NT - 1])
                if L0:
                    for c in range(CT):
                        lower(h0T_lo[:, c, :], ps_B[:, c, :], h0T_hi[:, c, :], h0T_hi_done[c], h0T_lo_done[c], L0,
                              s2_done)
                if L1:
                    for c in range(CT):
                        lower(tT_lo[:, c, :], ps_C[:, c, :], tT_hi[:, c, :], tT_hi_done[c], tT_lo_done[c], L1,
                              rel_mm_done[NT - 1])
                for t in range(NT):
                    if L0:
                        masked_max(t, L0)
                    if L1:
                        rel_mask(t, L1)
                    if L0 and t:
                        softmax_scale(t - 1, L0)
                if L0:
                    softmax_scale(NT - 1, L0)
                if nxt:
                    statistics0(nxt)
                if L0:
                    for t in range(NT):
                        lower(attT_lo[:, :, t * P:(t + 1) * P], attT_ps[t].rearrange("p (j n) -> p j n", j=NT),
                              attT_hi[:, :, t * P:(t + 1) * P], attT_hi_done[t],
                              attT_lo_done if t == NT - 1 else None, L0, mix_done[CT - 1])
                    for c in range(CT):
                        lower(mixT_lo[:, c, :], ps_A[:, c, :], mixT_hi[:, c, :], mixT_hi_done[c], mixT_lo_done[c], L0,
                              y_done[1])
                if L1:
                    lower(aggT_lo[:, 0, :], ps_B[:, 0, :], aggT_hi[:, 0, :], aggT_hi_done[0], aggT_lo_done[0], L1,
                          out_done[1])
                if L0:
                    wait(dve, xres_in, L0.dma_now)
                    wait(dve, g_done[NT - 1], L0.before)
                    wait(dve, x1_done, L0.before)
                    for c in range(2):
                        wait(dve, exp_y_done[c], L0.now)
                        dve.scalar_tensor_tensor(out=elu_x[:, 2 * c:2 * c + 2, :], in0=exp_y[:, 2 * c:2 * c + 2, :],
                                                 scalar=1.0, in1=x_res[:, 2 * c:2 * c + 2, :], op0=ALU.min,
                                                 op1=ALU.add).then_inc(elu_x_done[c], 1)
                        wait(dve, elu_x_done[c], L0.now)
                        dve.scalar_tensor_tensor(out=x1p[:, 2 * c:2 * c + 2, :],
                                                 in0=ps_C[:, c, :].rearrange("p (t c) -> p t c", t=2),
                                                 scalar=0.0, in1=elu_x[:, 2 * c:2 * c + 2, :], op0=ALU.max,
                                                 op1=ALU.add).then_inc(x1p_done[c], 1)
                if L1:
                    lower(aggT_lo[:, 1, :], ps_B[:, 1, :], aggT_hi[:, 1, :], aggT_hi_done[1], aggT_lo_done[1], L1)
                if L0:
                    wait(dve, x1p_done[1], L0.now)
                    statistics(x1p, bn1, mom1, bn1_done, mom1_done, rstd1_done, L0)
                if nxt:
                    upper_h0(nxt)
                    score1(nxt)
                if L1:
                    wait(dve, inv_norm_done, L1.before)
                    wait(dve, norm_mm_done, L1.now)
                    dve.tensor_copy(norm_sq[:], norm_ps).then_inc(norm_copied, 1)
                    wait(dve, stored, L1.dma_before)
                    wait(dve, x1_done, L1.now)
                    wait(dve, inv_norm_done, L1.now)
                    for t in range(NT):
                        if t % 2 == 0:
                            wait(dve, out_done[t // 2], L1.now)
                        ins = dve.scalar_tensor_tensor(out=y_out[:, t, :], in0=rows(ps_D, t),
                                                       scalar=inv_norm[:, t:t + 1], in1=x1[:, t, :], op0=ALU.mult,
                                                       op1=ALU.add)
                        if t % 2:
                            ins.then_inc(out_added[t // 2], 1)
                if L0:
                    wait(dve, agg_done[CT - 1], L0.before)
                    wait(dve, g_lo_done, L0.before)
                    wait(dve, g_done[NT - 1], L0.now)
                    dve.tensor_copy(g_hi[:], g[:]).then_inc(g_hi_done, 1)

            statistics0(graph(0))
            upper_h0(graph(0))

            dve.wait_ge(consts_made, 3)
            dve.wait_ge(weights_in, 6 * DMA)
            for t in range(2 * CT):
                dve.tensor_scalar(a_rep[:, t, :], ones[:], a_col[:, t:t + 1], None, ALU.mult).then_inc(a_spread, 1)
            dve.wait_ge(turned, 1)
            dve.tensor_copy(WT, ps_A[:, 0, :].rearrange("p (t c) -> p t c", t=CT)).then_inc(turned_copied, 1)
            dve.tensor_copy(beta_sb[:], ps_C[:, 1, 0:1]).then_inc(setup_chain, 1)
            dve.wait_ge(setup_chain, 1)
            dve.tensor_scalar(beta_ident[:], ident[:], beta_sb[:], None, ALU.mult).then_inc(setup_chain, 1)
            dve.wait_ge(made, 1)
            dve.tensor_copy(wa1_rows[:], ps_B[:, 0, 0:C]).then_inc(setup_chain, 1)
            splits = [(W_hi, W_lo, W_in),
                      (WvT_hi, WvT_lo, ps_A[:, 1, :].rearrange("p (t c) -> p t c", t=CT)),
                      (G_hi, G_lo, ps_C[:, 0, :].rearrange("p (t c) -> p t c", t=CT)),
                      (wa2_hi, wa2_lo, ps_B[:, 1, 0:CT * P].rearrange("p (t c) -> p t c", t=CT))]
            for hi, _, src in splits:
                dve.tensor_copy(hi[:], src).then_inc(setup_chain, 1)
            dve.wait_ge(setup_chain, 3 + len(splits))
            for hi, lo, src in splits:
                last = dve.tensor_tensor(lo[:], src, hi[:].bitcast(F32), ALU.subtract)
            last.then_inc(setup_done, 1)
            dve.wait_ge(setup_done, 1)
            score1(graph(0))
            run_steps(dve, B, step)

        @block.tensor
        def _(pe):
            pe.wait_ge(weights_in, 6 * DMA)
            pe.wait_ge(consts_made, 3)
            for src, bank in ((W_in, 0), (Wv_in, 1)):
                for r in range(CT):
                    for c in range(CT):
                        pe.transpose(ps_A[:, bank, c * C + r * P:c * C + (r + 1) * P],
                                     src[:, r, c * P:(c + 1) * P], ident[:])
            pe.matmul(ps_C[:, 1, 0:1], ones[0:1, :], beta_row, start=True, stop=True).then_inc(turned, 1)
            pe.wait_ge(a_spread, 2 * CT)
            pe.wait_ge(turned_copied, 1)
            for t in range(CT):
                pe.matmul(ps_B[:, 0, 0:C], a_rep[:, t, :], WT[:, t, :], start=t == 0, stop=t == CT - 1)
            for c in range(CT):
                for t in range(CT):
                    pe.matmul(ps_B[:, 1, c * P:(c + 1) * P], WT[:, t, c * P:(c + 1) * P], a_rep[:, CT + t, :],
                              start=t == 0, stop=t == CT - 1)
            for c in range(CT):
                for t in range(CT):
                    mm = pe.matmul(ps_C[:, 0, c * C:(c + 1) * C], Wq_in[:, t, c * P:(c + 1) * P], Wk_in[:, t, :],
                                   start=t == 0, stop=t == CT - 1)
            mm.then_inc(made, 1)
            pe.wait_ge(setup_done, 1)

            def product(dst, lhs, rhs, before_lo=None):
                n = len(lhs)
                for k in range(n):
                    pe.matmul(dst, lhs[k][0], rhs[k][0], start=k == 0, stop=False)
                if before_lo:
                    before_lo()
                for k in range(n):
                    pe.matmul(dst, lhs[k][0], rhs[k][1], start=False, stop=False)
                    mm = pe.matmul(dst, lhs[k][1], rhs[k][0], start=False, stop=k == n - 1)
                return mm

            def turn(src, src_done, pair_of_banks, done, b):
                for t in range(NT):
                    wait(pe, src_done[t], b.now)
                    for c in range(CT):
                        tr = pe.transpose(pair_of_banks[:, c, t * P:(t + 1) * P], src[:, t, c * P:(c + 1) * P],
                                          ident[:])
                        if t == NT - 1:
                            tr.then_inc(done[c], 1)

            def both(hi, lo, *where):
                return hi[(slice(None), *where)], lo[(slice(None), *where)]

            def cols(t):
                return slice(t * P, (t + 1) * P)

            def turn_g(b):
                wait(pe, norm_copied, b.before)
                turn(g, g_done, ps_A, g_turned, b)

            def scores2(b):
                for c in range(CT):
                    wait(pe, h0T_lo_done[c], b.now)
                wait(pe, out_added[0], b.before_l1)
                product(ps_D[:, 0, :], [both(wa2_hi, wa2_lo, c) for c in range(CT)],
                        [both(h0T_hi, h0T_lo, c) for c in range(CT)]).then_inc(s2_done, 1)

            def t_product(b):
                for c in range(CT):
                    wait(pe, gT_lo_done[c], b.now)
                for c in range(CT):
                    product(ps_C[:, c, :], [both(G_hi, G_lo, k, cols(c)) for k in range(CT)],
                            [both(gT_hi, gT_lo, k) for k in range(CT)]).then_inc(t_done[c], 1)

            def rel_product(b):
                for c in range(CT):
                    wait(pe, tT_lo_done[c], b.now)
                for t in range(NT):
                    product(rel_ps[t], [both(gT_hi, gT_lo, k, cols(t)) for k in range(CT)],
                            [both(tT_hi, tT_lo, k) for k in range(CT)]).then_inc(rel_mm_done[t], 1)

            def turn_att(b):
                for t in range(NT):
                    if t == 2:
                        wait(pe, out_added[1], b.before_l1)
                    wait(pe, att_done[t], b.now)
                    for j in range(NT):
                        tr = pe.transpose(attT_ps[t][:, cols(j)], att[:, t, cols(j)], ident[:])
                    tr.then_inc(att_turned[t], 1)

            def mix(b, L1):
                wait(pe, h0_lo_done, b.now)
                wait(pe, attT_lo_done, b.now)
                if L1:
                    for t in range(CT):
                        wait(pe, rel_done[t], L1.now)
                for c in range(CT):
                    product(ps_A[:, c, :], [both(h0_hi, h0_lo, j, cols(c)) for j in range(NT)],
                            [both(attT_hi, attT_lo, j) for j in range(NT)]).then_inc(mix_done[c], 1)

            def y_product(b):
                for c in range(CT):
                    wait(pe, mixT_lo_done[c], b.now)
                for t in range(NT):
                    mm = product(rows(ps_C, t), [both(mixT_hi, mixT_lo, k, cols(t)) for k in range(CT)],
                                 [both(W_hi, W_lo, k) for k in range(CT)])
                    if t % 2:
                        mm.then_inc(y_done[t // 2], 1)

            def aggregate(b, c):
                if c == 0:
                    wait(pe, g_lo_done, b.now)
                    for t in range(NT):
                        wait(pe, rel_lo_done[t], b.now)
                product(ps_B[:, c, :], [both(g_hi, g_lo, j, cols(c)) for j in range(NT)],
                        [both(rel_hi, rel_lo, j) for j in range(NT)]).then_inc(agg_done[c], 1)

            def norms(b):
                wait(pe, sum_sq_done[NT - 2], b.now)
                for t in range(NT):
                    mm = pe.matmul(norm_ps[:, t:t + 1], sum_sq[:, cols(t)], ones[:, 0:1], start=True, stop=True)
                mm.then_inc(norm_mm_done, 1)

            def out_product(b):
                for c in range(CT):
                    wait(pe, aggT_lo_done[c], b.now)
                for t in range(NT):
                    mm = product(rows(ps_D, t), [both(aggT_hi, aggT_lo, k, cols(t)) for k in range(CT)],
                                 [both(WvT_hi, WvT_lo, k) for k in range(CT)])
                    if t % 2:
                        mm.then_inc(out_done[t // 2], 1)

            def step(L0, L1, nxt):
                if L1:
                    turn_g(L1)
                if L0:
                    L0.before_l1 = L1.before if L1 else 0
                    turn(h0, h0_done, ps_B, h0_turned, L0)
                if L1:
                    t_product(L1)
                if L0:
                    scores2(L0)
                if L1:
                    rel_product(L1)
                if L0:
                    turn_att(L0)
                    mix(L0, L1)
                if L1:
                    aggregate(L1, 0)
                if L0:
                    y_product(L0)
                if L1:
                    aggregate(L1, 1)
                    norms(L1)
                    out_product(L1)

            run_steps(pe, B, step)


_INS = ["x", "adj", "L0_gnn_W", "L0_gnn_a", "L0_gnn_beta", "L1_gnn_Wq", "L1_gnn_Wk", "L1_gnn_Wv"]


def kernel(**inputs):
    import numpy as np
    import concourse.bacc as bacc
    from concourse.bass_utils import run_bass_kernel_spmd

    nc = bacc.Bacc("TRN2", target_bir_lowering=False, num_devices=1)
    arrays, args = {}, []
    for name in _INS:
        v = np.ascontiguousarray(inputs[name])
        arrays[f"in_{name}"] = v
        args.append(nc.dram_tensor(f"in_{name}", v.shape, mybir.dt.from_np(v.dtype), kind="ExternalInput").ap())
    out = nc.dram_tensor("out", inputs["x"].shape, F32, kind="ExternalOutput").ap()
    build(nc, *args, out)
    result = run_bass_kernel_spmd(nc, [arrays], core_ids=[0])
    return result.results[0]["out"]
```

```python
from contextlib import ExitStack

import concourse.bass as bass
from concourse import mybir

F32 = mybir.dt.float32
F32R = mybir.dt.float32r
ALU = mybir.AluOpType
ACT = mybir.ActivationFunctionType

P = 128
LEAK = 0.2
EPS = 1e-5
LOWEST = -3.4028235e38
DMA = 16


class Graph:

    def __init__(self, now, before, index=None, dma_now=None, dma_before=None):
        self.now, self.before, self.index = now, before, index
        self.dma_now, self.dma_before = dma_now, dma_before


def graph(b):
    return Graph(b + 1, b, b, DMA * (b + 1), DMA * b)


def wait(eng, sem, count):
    if not (isinstance(count, int) and count <= 0):
        eng.wait_ge(sem, count)


def run_steps(eng, B, step):
    def peeled(i):
        step(*(graph(b) if 0 <= b < B else None for b in range(i - 1, i + 3)))

    peeled(0)
    peeled(1)
    with eng.Fori(2, B - 2) as i:
        counts = [eng.snap(i + n) for n in range(-1, 4)]
        dma_counts = [eng.snap(n * DMA) for n in counts]
        for count in counts + dma_counts:
            eng.compute_val(count)
        step(*(Graph(counts[k + 1], counts[k], counts[k], dma_counts[k + 1], dma_counts[k]) for k in range(4)))
    for i in range(B - 2, B + 1):
        peeled(i)


def build(nc, x, adj, W, a, beta, Wq, Wk, Wv, out):
    B, N, C = x.shape
    NT, CT = N // P, C // P
    assert N == 512 and C == 256 and W.shape == (C, C)

    with ExitStack() as ctx:
        def sb(name, shape, dt=F32):
            return ctx.enter_context(nc.sbuf_tensor(name, [P, *shape], dt))

        def sem(name):
            return ctx.enter_context(nc.semaphore(name))

        def sems(name, n):
            return [sem(f"{name}_{t}") for t in range(n)]

        def pair(name, shape):
            return sb(name + "_hi", shape, F32R), sb(name + "_lo", shape, F32R)

        ident = sb("ident", [P])
        ones = sb("ones", [P])
        adj_sb = sb("adj_sb", [NT, N])
        minus_half = sb("minus_half", [NT])
        beta_sb = sb("beta_sb", [1])
        beta_ident = sb("beta_ident", [P])
        wa1_rows = sb("wa1_rows", [C])
        W_hi, W_lo = pair("W", [CT, C])
        G_hi, G_lo = pair("G", [CT, C])
        WvT_hi, WvT_lo = pair("WvT", [CT, C])
        wa2_hi, wa2_lo = pair("wa2", [CT, P])

        x_sb = sb("x_sb", [NT, C])
        x_res = sb("x_res", [NT, C])
        bn0 = sb("bn0", [NT, 6])
        mom0 = sb("mom0", [NT, 2])
        rstd0 = sb("rstd0", [NT])
        bias0 = sb("bias0", [NT])
        small0 = sb("small0", [2, NT])
        h0 = sb("h0", [NT, C])
        h0_hi, h0_lo = pair("h0", [NT, C])
        h0T_hi, h0T_lo = pair("h0T", [CT, N])
        s1 = sb("s1", [NT])
        s1_products = sb("s1_products", [NT, C])
        z = sb("z", [NT, N])
        e = sb("e", [NT, N])
        att = sb("att", [NT, N])
        row_max = sb("row_max", [NT])
        minus_max = sb("minus_max", [NT])
        row_sum = sb("row_sum", [NT])
        row_inv = sb("row_inv", [NT])
        attT_hi, attT_lo = pair("attT", [NT, N])
        mixT_hi, mixT_lo = pair("mixT", [CT, N])
        exp_y = sb("exp_y", [NT, C])
        elu_x = sb("elu_x", [NT, C])
        x1p = sb("x1p", [NT, C])

        x1 = sb("x1", [NT, C])
        bn1 = sb("bn1", [NT, 6])
        mom1 = sb("mom1", [NT, 2])
        rstd1 = sb("rstd1", [NT])
        bias1 = sb("bias1", [NT])
        small1 = sb("small1", [2, NT])
        g = sb("g", [NT, C])
        g_hi, g_lo = pair("g", [NT, C])
        gT_hi, gT_lo = pair("gT", [CT, N])
        tT_hi, tT_lo = pair("tT", [CT, N])
        rel = sb("rel", [NT, N])
        rel_hi, rel_lo = pair("rel", [NT, N])
        squares = sb("squares", [NT, N])
        sum_sq = sb("sum_sq", [N])
        aggT_hi, aggT_lo = pair("aggT", [CT, N])
        norm_sq = sb("norm_sq", [NT])
        inv_norm = sb("inv_norm", [NT])
        y_out = sb("y_out", [NT, C])

        W_in, Wq_in, Wk_in, Wv_in = (z[:, t, :].rearrange("p (t c) -> p t c", t=CT) for t in range(4))
        WT, a_rep = (e[:, t, :].rearrange("p (t c) -> p t c", c=c) for t, c in ((0, C), (1, P)))
        a_col = e[:, 2, 0:2 * CT]
        beta_row = e[0:1, 3, 0:1]

        ps_A, ps_B, ps_C, ps_D = (ctx.enter_context(nc.psum_tensor(f"ps_{n}", [P, 2, N], F32)) for n in "ABCD")
        s2_ps = ps_B[:, 0, :]
        norm_ps = ps_C[:, 0, 0:NT]
        rel_ps = [ps_A[:, 0, :], ps_A[:, 1, :], ps_B[:, 0, :], ps_B[:, 1, :]]
        attT_ps = [ps_D[:, 0, :], ps_D[:, 1, :], ps_A[:, 0, :], ps_A[:, 1, :]]

        def rows(pair_of_banks, t):
            return pair_of_banks[:, t // 2, (t % 2) * C:(t % 2 + 1) * C]

        weights_in = sem("weights_in")
        adj_in = sem("adj_in")
        zeroed = sem("zeroed")
        consts_made = sem("consts_made")
        a_spread = sem("a_spread")
        turned = sem("turned")
        turned_copied = sem("turned_copied")
        made = sem("made")
        setup_chain = sem("setup_chain")
        setup_done = sem("setup_done")

        x_in, xres_in = sem("x_in"), sem("xres_in")
        bn0_done, mom0_done = sem("bn0_done"), sem("mom0_done")
        var0_done, rstd0_done, bias0_done = sem("var0_done"), sem("rstd0_done"), sem("bias0_done")
        h0_done = sem("h0_done")
        h0_hi_done, h0_lo_done = sem("h0_hi_done"), sem("h0_lo_done")
        h0_turned = sems("h0_turned", CT)
        h0T_hi_done, h0T_lo_done = sems("h0T_hi_done", CT), sems("h0T_lo_done", CT)
        s1_done = sems("s1_done", NT)
        s2_done = sem("s2_done")
        z_done, leaky_done = sems("z_done", NT), sems("leaky_done", NT)
        e_done, max_done = sems("e_done", NT), sems("max_done", NT)
        exp_done, inv_done = sems("exp_done", NT), sems("inv_done", NT)
        scaled, att_done = sems("scaled", NT), sems("att_done", NT)
        att_turned = sems("att_turned", NT)
        attT_hi_done, attT_lo_done = sems("attT_hi_done", NT), sem("attT_lo_done")
        mix_done = sems("mix_done", CT)
        mixT_hi_done, mixT_lo_done = sems("mixT_hi_done", CT), sems("mixT_lo_done", CT)
        y_done, exp_y_done = sems("y_done", 2), sems("exp_y_done", 2)
        elu_x_done, x1p_done = sems("elu_x_done", 2), sems("x1p_done", 2)

        x1_done = sem("x1_done")
        bn1_done, mom1_done = sems("bn1_done", 2), sems("mom1_done", 2)
        var1_done, rstd1_done, bias1_done = sems("var1_done", 2), sems("rstd1_done", 2), sems("bias1_done", 2)
        g_done = sems("g_done", 2)
        g_hi_done, g_lo_done = sem("g_hi_done"), sem("g_lo_done")
        g_turned = sems("g_turned", CT)
        gT_hi_done, gT_lo_done = sems("gT_hi_done", CT), sems("gT_lo_done", CT)
        t_done = sems("t_done", CT)
        tT_hi_done, tT_lo_done = sems("tT_hi_done", CT), sems("tT_lo_done", CT)
        rel_mm_done, rel_done = sems("rel_mm_done", NT), sems("rel_done", NT)
        rel_hi_done, rel_lo_done = sems("rel_hi_done", NT), sems("rel_lo_done", NT)
        squared, sum_sq_done = sems("squared", NT), sems("sum_sq_done", NT - 1)
        agg_done = sems("agg_done", CT)
        aggT_hi_done, aggT_lo_done = sems("aggT_hi_done", CT), sems("aggT_lo_done", CT)
        norm_mm_done, norm_copied, inv_norm_done = sem("norm_mm_done"), sem("norm_copied"), sem("inv_norm_done")
        out_done = sems("out_done", 2)
        out_added = sems("out_added", 2)
        stored = sem("stored")

        def tiled(w):
            return w.rearrange("(t p) c -> p t c", p=P)

        block = ctx.enter_context(nc.Block())

        @block.sync
        def _(sp):
            sp.dma_start(x_sb[:], tiled(x[0])).then_inc(x_in, DMA)
            for dst, src in ((W_in, W), (Wq_in, Wq), (Wk_in, Wk), (Wv_in, Wv)):
                sp.dma_start(dst, tiled(src)).then_inc(weights_in, DMA)
            with nc.allow_non_contiguous_dma(reason="the 512 numbers of a, once"):
                sp.dma_start(a_col, a.rearrange("(t p) o -> p (t o)", p=P)).then_inc(weights_in, DMA)
            sp.dma_start(beta_row, beta.rearrange("(o n) -> o n", o=1)).then_inc(weights_in, DMA)
            sp.dma_start(adj_sb[:], tiled(adj)).then_inc(adj_in, DMA)
            sp.dma_start(x_res[:], tiled(x[0])).then_inc(xres_in, DMA)

            def load_x(b):
                wait(sp, h0_done, b.before)
                sp.dma_start(x_sb[:], tiled(x[b.index])).then_inc(x_in, DMA)

            load_x(graph(1))

            def step(last, cur, nxt, later):
                if later:
                    load_x(later)
                if nxt:
                    wait(sp, elu_x_done[1], nxt.before)
                    sp.dma_start(x_res[:], tiled(x[nxt.index])).then_inc(xres_in, DMA)
                if last:
                    wait(sp, out_added[1], last.now)
                    sp.dma_start(tiled(out[last.index]), y_out[:]).then_inc(stored, DMA)

            run_steps(sp, B, step)
            sp.wait_ge(stored, DMA * B)

        @block.gpsimd
        def _(pool):
            pool.memset(ident[:], 0.0).then_inc(zeroed, 1)
            pool.memset(ones[:], 1.0).then_inc(consts_made, 1)
            pool.memset(minus_half[:], -0.5).then_inc(consts_made, 1)
            pool.wait_ge(zeroed, 1)
            pool.affine_select(out=ident[:], in_=ident[:], compare_op=ALU.not_equal, fill=1.0, base=0,
                               pattern=[[-1, P]], channel_multiplier=1).then_inc(consts_made, 1)
            pool.wait_ge(consts_made, 3)

            def moments(mom, small, rstd, bias, tiles, mom_done, var_done, rstd_done, bias_done, h_done, b):
                pool.wait_ge(consts_made, 3)
                wait(pool, h_done, b.before)
                wait(pool, mom_done, b.now)
                pool.tensor_scalar(small[:, 0, tiles], mom[:, tiles, 1], 1.0, EPS, ALU.mult, ALU.add)
                pool.tensor_scalar(small[:, 1, tiles], mom[:, tiles, 0], -1.0, 0.0, ALU.mult,
                                   ALU.add).then_inc(var_done, 1)
                wait(pool, var_done, b.now)
                pool.tensor_tensor(rstd[:, tiles], small[:, 0, tiles], minus_half[:, tiles],
                                   ALU.pow).then_inc(rstd_done, 1)
                wait(pool, rstd_done, b.now)
                pool.tensor_tensor(bias[:, tiles], small[:, 1, tiles], rstd[:, tiles], ALU.mult).then_inc(bias_done, 1)

            def moments0(b):
                moments(mom0, small0, rstd0, bias0, slice(0, NT), mom0_done, var0_done, rstd0_done, bias0_done,
                        h0_done, b)

            def moments1(half, b):
                moments(mom1, small1, rstd1, bias1, slice(2 * half, 2 * half + 2), mom1_done[half], var1_done[half],
                        rstd1_done[half], bias1_done[half], g_done[half], b)

            def h0_low(b):
                wait(pool, mix_done[CT - 1], b.before)
                wait(pool, h0_hi_done, b.now)
                pool.tensor_tensor(h0_lo[:], h0[:], h0_hi[:].bitcast(F32), ALU.subtract).then_inc(h0_lo_done, 1)

            def g_low(b):
                wait(pool, agg_done[CT - 1], b.before)
                wait(pool, g_hi_done, b.now)
                pool.tensor_tensor(g_lo[:], g[:], g_hi[:].bitcast(F32), ALU.subtract).then_inc(g_lo_done, 1)

            def add_beta(t, b):
                wait(pool, scaled[t], b.now)
                d = att[:, t, t * P:(t + 1) * P]
                pool.tensor_tensor(d, d, beta_ident[:], ALU.add).then_inc(att_done[t], 1)

            def rel_low(t, b):
                wait(pool, agg_done[CT - 1], b.before)
                wait(pool, rel_hi_done[t], b.now)
                pool.tensor_tensor(rel_lo[:, t, :], rel[:, t, :], rel_hi[:, t, :].bitcast(F32),
                                   ALU.subtract).then_inc(rel_lo_done[t], 1)

            def sum_squares(b):
                wait(pool, norm_mm_done, b.before)
                for t in range(1, NT):
                    wait(pool, squared[t], b.now)
                    if t > 1:
                        wait(pool, sum_sq_done[t - 2], b.now)
                    pool.tensor_tensor(sum_sq[:], squares[:, 0, :] if t == 1 else sum_sq[:], squares[:, t, :],
                                       ALU.add).then_inc(sum_sq_done[t - 1], 1)

            def step(last, cur, nxt, later):
                if last:
                    rel_low(2, last)
                    rel_low(3, last)
                if later:
                    moments0(later)
                if nxt:
                    h0_low(nxt)
                    add_beta(0, nxt)
                if last:
                    sum_squares(last)
                if cur:
                    moments1(0, cur)
                if last:
                    wait(pool, norm_copied, last.now)
                    pool.tensor_tensor(inv_norm[:], norm_sq[:], minus_half[:], ALU.pow).then_inc(inv_norm_done, 1)
                if cur:
                    moments1(1, cur)
                if nxt:
                    add_beta(1, nxt)
                if cur:
                    pool.wait_ge(consts_made, 3)
                    wait(pool, out_added[1], cur.before)
                    wait(pool, x1p_done[1], cur.now)
                    pool.tensor_scalar(x1[:], x1p[:], 1.0, -1.0, ALU.mult, ALU.add).then_inc(x1_done, 1)
                    g_low(cur)
                if nxt:
                    add_beta(2, nxt)
                    add_beta(3, nxt)
                if cur:
                    rel_low(0, cur)
                    rel_low(1, cur)

            moments0(graph(0))
            h0_low(graph(0))
            moments0(graph(1))
            pool.wait_ge(setup_done, 1)
            for t in range(NT):
                add_beta(t, graph(0))
            run_steps(pool, B, step)

        @block.scalar
        def _(act):
            def upper(dst, src, ready, done, b, reader=None):
                if reader:
                    wait(act, reader, b.before)
                wait(act, ready, b.now)
                act.activation(dst, src, ACT.Copy).then_inc(done, 1)

            def normalise(dst, src, rstd, bias, tiles, bias_done, done, b):
                wait(act, bias_done, b.now)
                for t in tiles:
                    ins = act.activation(dst[:, t, :], src[:, t, :], ACT.Relu, bias=bias[:, t:t + 1],
                                         scale=rstd[:, t:t + 1])
                ins.then_inc(done, 1)

            def normalise0(b):
                wait(act, h0_turned[CT - 1], b.before)
                wait(act, s1_done[NT - 1], b.before)
                wait(act, h0_lo_done, b.before)
                normalise(h0, x_sb, rstd0, bias0, range(NT), bias0_done, h0_done, b)

            def normalise1(half, b):
                wait(act, g_turned[CT - 1], b.before)
                wait(act, g_lo_done, b.before)
                normalise(g, x1p, rstd1, bias1, range(2 * half, 2 * half + 2), bias1_done[half], g_done[half], b)

            def upper_h0(b):
                wait(act, mix_done[CT - 1], b.before)
                wait(act, h0_lo_done, b.before)
                wait(act, h0_done, b.now)
                act.activation(h0_hi[:], h0[:], ACT.Copy).then_inc(h0_hi_done, 1)

            def upper_h0T(b):
                for c in range(CT):
                    upper(h0T_hi[:, c, :], ps_B[:, c, :], h0_turned[c], h0T_hi_done[c], b, s2_done)

            def scores(b):
                wait(act, s2_done, b.now)
                for t in range(NT):
                    wait(act, leaky_done[t], b.before)
                    wait(act, s1_done[t], b.now)
                    act.activation(z[:, t, :], s2_ps, ACT.Identity, bias=s1[:, t:t + 1]).then_inc(z_done[t], 1)

            def exponent(t, b):
                wait(act, att_turned[t], b.before)
                wait(act, inv_done[t], b.before)
                wait(act, max_done[t], b.now)
                act.activation(att[:, t, :], e[:, t, :], ACT.Exp, bias=minus_max[:, t:t + 1],
                               accum_out=row_sum[:, t:t + 1]).then_inc(exp_done[t], 1)

            def exp_of_y(half, b):
                wait(act, elu_x_done[half], b.before)
                wait(act, y_done[half], b.now)
                act.activation(exp_y[:, 2 * half:2 * half + 2, :],
                               ps_A[:, half, :].rearrange("p (t c) -> p t c", t=2), ACT.Exp).then_inc(exp_y_done[half], 1)

            def upper_rel(t, b):
                wait(act, agg_done[CT - 1], b.before)
                wait(act, rel_done[t], b.now)
                act.activation(rel_hi[:, t, :], rel[:, t, :], ACT.Copy).then_inc(rel_hi_done[t], 1)

            def square(t, b):
                wait(act, rel_done[t], b.now)
                wait(act, sum_sq_done[NT - 2], b.before)
                act.activation(squares[:, t, :], rel[:, t, :], ACT.Square).then_inc(squared[t], 1)

            def step(last, cur, nxt, later):
                if cur:
                    for t in range(NT):
                        upper(attT_hi[:, :, t * P:(t + 1) * P], attT_ps[t].rearrange("p (j n) -> p j n", j=NT),
                              att_turned[t], attT_hi_done[t], cur, mix_done[CT - 1])
                if last:
                    upper_rel(2, last)
                    upper_rel(3, last)
                if nxt:
                    scores(nxt)
                if cur:
                    upper(mixT_hi[:, 0, :], ps_C[:, 0, :], mix_done[0], mixT_hi_done[0], cur, y_done[1])
                if nxt:
                    exponent(0, nxt)
                if cur:
                    upper(mixT_hi[:, 1, :], ps_C[:, 1, :], mix_done[1], mixT_hi_done[1], cur)
                if nxt:
                    upper_h0(nxt)
                if last:
                    square(0, last)
                    square(1, last)
                if nxt:
                    exponent(1, nxt)
                if cur:
                    exp_of_y(0, cur)
                if last:
                    square(2, last)
                if cur:
                    exp_of_y(1, cur)
                if last:
                    square(3, last)
                    upper(aggT_hi[:, 0, :], ps_D[:, 0, :], agg_done[0], aggT_hi_done[0], last, out_done[1])
                if last:
                    upper(aggT_hi[:, 1, :], ps_D[:, 1, :], agg_done[1], aggT_hi_done[1], last)
                if later:
                    normalise0(later)
                if cur:
                    normalise1(0, cur)
                    normalise1(1, cur)
                if nxt:
                    exponent(2, nxt)
                if cur:
                    for c in range(CT):
                        upper(gT_hi[:, c, :], ps_D[:, c, :], g_turned[c], gT_hi_done[c], cur, rel_mm_done[NT - 1])
                if later:
                    upper_h0T(later)
                if cur:
                    for c in range(CT):
                        upper(tT_hi[:, c, :], ps_C[:, c, :], t_done[c], tT_hi_done[c], cur, rel_mm_done[NT - 1])
                if nxt:
                    exponent(3, nxt)
                if cur:
                    wait(act, agg_done[CT - 1], cur.before)
                    wait(act, g_lo_done, cur.before)
                    act.activation(g_hi[:], g[:], ACT.Copy).then_inc(g_hi_done, 1)
                    upper_rel(0, cur)
                    upper_rel(1, cur)

            normalise0(graph(0))
            upper_h0(graph(0))
            upper_h0T(graph(0))
            scores(graph(0))
            normalise0(graph(1))
            for t in range(NT):
                exponent(t, graph(0))
            upper_h0T(graph(1))
            run_steps(act, B, step)

        @block.vector
        def _(dve):
            def lower(dst, src, hi, hi_done, done, b, reader=None):
                if reader:
                    wait(dve, reader, b.before)
                wait(dve, hi_done, b.now)
                ins = dve.tensor_tensor(dst, src, hi.bitcast(F32), ALU.subtract)
                if done:
                    ins.then_inc(done, 1)

            def statistics(src, bn, mom, tiles, bn_done, mom_done, rstd_done, b):
                for t in tiles:
                    ins = dve.bn_stats(bn[:, t, :], src[:, t, :])
                ins.then_inc(bn_done, 1)
                dve.wait_ge(x_in, DMA)
                wait(dve, rstd_done, b.before)
                wait(dve, bn_done, b.now)
                for t in tiles:
                    ins = dve.bn_aggr(mom[:, t, :], bn[:, t, :])
                ins.then_inc(mom_done, 1)

            def statistics0(b):
                wait(dve, mom0_done, b.before)
                wait(dve, x_in, b.dma_now)
                statistics(x_sb, bn0, mom0, range(NT), bn0_done, mom0_done, rstd0_done, b)

            def statistics1(half, b):
                wait(dve, mom1_done[half], b.before)
                wait(dve, x1p_done[half], b.now)
                statistics(x1p, bn1, mom1, range(2 * half, 2 * half + 2), bn1_done[half], mom1_done[half],
                           rstd1_done[half], b)

            def score1(b, tiles=range(NT)):
                for t in tiles:
                    wait(dve, z_done[t], b.before)
                    wait(dve, h0_done, b.now)
                    dve.wait_ge(adj_in, DMA)
                    dve.tensor_tensor_reduce(s1_products[:, t, :], h0[:, t, :], wa1_rows[:], 1.0, 0.0, ALU.mult, ALU.add,
                                             s1[:, t:t + 1]).then_inc(s1_done[t], 1)

            def masked_max(t, b):
                wait(dve, exp_done[t], b.before)
                wait(dve, z_done[t], b.now)
                dve.scalar_tensor_tensor(out=e[:, t, :], in0=z[:, t, :], scalar=LEAK, in1=z[:, t, :], op0=ALU.mult,
                                         op1=ALU.max).then_inc(leaky_done[t], 1)
                dve.wait_ge(adj_in, DMA)
                wait(dve, leaky_done[t], b.now)
                dve.tensor_tensor_reduce(e[:, t, :], e[:, t, :], adj_sb[:, t, :], 1.0, LOWEST, ALU.mult, ALU.max,
                                         row_max[:, t:t + 1]).then_inc(e_done[t], 1)
                wait(dve, e_done[t], b.now)
                dve.tensor_scalar(minus_max[:, t:t + 1], row_max[:, t:t + 1], -1.0, None,
                                  ALU.mult).then_inc(max_done[t], 1)

            def softmax_scale(t, b):
                wait(dve, exp_done[t], b.now)
                dve.reciprocal(row_inv[:, t:t + 1], row_sum[:, t:t + 1]).then_inc(inv_done[t], 1)
                wait(dve, inv_done[t], b.now)
                dve.tensor_scalar(att[:, t, :], att[:, t, :], row_inv[:, t:t + 1], None,
                                  ALU.mult).then_inc(scaled[t], 1)

            def rel_mask(t, b):
                wait(dve, rel_lo_done[t], b.before)
                wait(dve, squared[t], b.before)
                wait(dve, rel_mm_done[t], b.now)
                dve.tensor_tensor(rel[:, t, :], rel_ps[t], adj_sb[:, t, :], ALU.mult).then_inc(rel_done[t], 1)

            def lower_h0T(b):
                for c in range(CT):
                    lower(h0T_lo[:, c, :], ps_B[:, c, :], h0T_hi[:, c, :], h0T_hi_done[c], h0T_lo_done[c], b, s2_done)

            def elu(half, b):
                tiles = slice(2 * half, 2 * half + 2)
                wait(dve, g_done[1], b.before)
                wait(dve, x1_done, b.before)
                wait(dve, xres_in, b.dma_now)
                wait(dve, exp_y_done[half], b.now)
                dve.scalar_tensor_tensor(out=elu_x[:, tiles, :], in0=exp_y[:, tiles, :], scalar=1.0,
                                         in1=x_res[:, tiles, :], op0=ALU.min, op1=ALU.add).then_inc(elu_x_done[half], 1)
                wait(dve, elu_x_done[half], b.now)
                dve.scalar_tensor_tensor(out=x1p[:, tiles, :], in0=ps_A[:, half, :].rearrange("p (t c) -> p t c", t=2),
                                         scalar=0.0, in1=elu_x[:, tiles, :], op0=ALU.max,
                                         op1=ALU.add).then_inc(x1p_done[half], 1)

            def copy_norms(b):
                wait(dve, inv_norm_done, b.before)
                wait(dve, norm_mm_done, b.now)
                dve.tensor_copy(norm_sq[:], norm_ps).then_inc(norm_copied, 1)

            def output(b):
                wait(dve, stored, b.dma_before)
                wait(dve, x1_done, b.now)
                wait(dve, inv_norm_done, b.now)
                for t in range(NT):
                    if t % 2 == 0:
                        wait(dve, out_done[t // 2], b.now)
                    ins = dve.scalar_tensor_tensor(out=y_out[:, t, :], in0=rows(ps_B, t), scalar=inv_norm[:, t:t + 1],
                                                   in1=x1[:, t, :], op0=ALU.mult, op1=ALU.add)
                    if t % 2:
                        ins.then_inc(out_added[t // 2], 1)

            def step(last, cur, nxt, later):
                if cur:
                    for t in range(NT):
                        lower(attT_lo[:, :, t * P:(t + 1) * P], attT_ps[t].rearrange("p (j n) -> p j n", j=NT),
                              attT_hi[:, :, t * P:(t + 1) * P], attT_hi_done[t],
                              attT_lo_done if t == NT - 1 else None, cur, mix_done[CT - 1])
                if later:
                    statistics0(later)
                if nxt:
                    masked_max(0, nxt)
                if cur:
                    lower(mixT_lo[:, 0, :], ps_C[:, 0, :], mixT_hi[:, 0, :], mixT_hi_done[0], mixT_lo_done[0], cur,
                          y_done[1])
                if cur:
                    lower(mixT_lo[:, 1, :], ps_C[:, 1, :], mixT_hi[:, 1, :], mixT_hi_done[1], mixT_lo_done[1], cur)
                if nxt:
                    masked_max(1, nxt)
                if nxt:
                    softmax_scale(0, nxt)
                if cur:
                    elu(0, cur)
                    elu(1, cur)
                if cur:
                    statistics1(0, cur)
                if last:
                    lower(aggT_lo[:, 0, :], ps_D[:, 0, :], aggT_hi[:, 0, :], aggT_hi_done[0], aggT_lo_done[0], last,
                          out_done[1])
                    lower(aggT_lo[:, 1, :], ps_D[:, 1, :], aggT_hi[:, 1, :], aggT_hi_done[1], aggT_lo_done[1], last)
                if last:
                    copy_norms(last)
                if cur:
                    statistics1(1, cur)
                if nxt:
                    masked_max(2, nxt)
                if last:
                    output(last)
                if nxt:
                    softmax_scale(1, nxt)
                if cur:
                    for c in range(CT):
                        lower(gT_lo[:, c, :], ps_D[:, c, :], gT_hi[:, c, :], gT_hi_done[c], gT_lo_done[c], cur,
                              rel_mm_done[NT - 1])
                if nxt:
                    masked_max(3, nxt)
                    softmax_scale(2, nxt)
                if cur:
                    for c in range(CT):
                        lower(tT_lo[:, c, :], ps_C[:, c, :], tT_hi[:, c, :], tT_hi_done[c], tT_lo_done[c], cur,
                              rel_mm_done[NT - 1])
                if later:
                    lower_h0T(later)
                if nxt:
                    softmax_scale(3, nxt)
                if cur:
                    rel_mask(0, cur)
                    rel_mask(1, cur)
                if later:
                    score1(later, range(2))
                if cur:
                    rel_mask(2, cur)
                    rel_mask(3, cur)
                if later:
                    score1(later, range(2, NT))

            statistics0(graph(0))

            dve.wait_ge(consts_made, 3)
            dve.wait_ge(weights_in, 6 * DMA)
            for t in range(2 * CT):
                dve.tensor_scalar(a_rep[:, t, :], ones[:], a_col[:, t:t + 1], None, ALU.mult).then_inc(a_spread, 1)
            dve.wait_ge(turned, 1)
            dve.tensor_copy(WT, ps_A[:, 0, :].rearrange("p (t c) -> p t c", t=CT)).then_inc(turned_copied, 1)
            dve.tensor_copy(beta_sb[:], ps_C[:, 1, 0:1]).then_inc(setup_chain, 1)
            dve.wait_ge(setup_chain, 1)
            dve.tensor_scalar(beta_ident[:], ident[:], beta_sb[:], None, ALU.mult).then_inc(setup_chain, 1)
            dve.wait_ge(made, 1)
            dve.tensor_copy(wa1_rows[:], ps_B[:, 0, 0:C]).then_inc(setup_chain, 1)
            splits = [(W_hi, W_lo, W_in),
                      (WvT_hi, WvT_lo, ps_A[:, 1, :].rearrange("p (t c) -> p t c", t=CT)),
                      (G_hi, G_lo, ps_C[:, 0, :].rearrange("p (t c) -> p t c", t=CT)),
                      (wa2_hi, wa2_lo, ps_B[:, 1, 0:CT * P].rearrange("p (t c) -> p t c", t=CT))]
            for hi, _, src in splits:
                dve.tensor_copy(hi[:], src).then_inc(setup_chain, 1)
            dve.wait_ge(setup_chain, 3 + len(splits))
            for hi, lo, src in splits:
                last = dve.tensor_tensor(lo[:], src, hi[:].bitcast(F32), ALU.subtract)
            last.then_inc(setup_done, 1)
            dve.wait_ge(setup_done, 1)
            lower_h0T(graph(0))
            score1(graph(0))
            statistics0(graph(1))
            for t in range(NT):
                masked_max(t, graph(0))
            for t in range(NT):
                softmax_scale(t, graph(0))
            lower_h0T(graph(1))
            score1(graph(1))
            run_steps(dve, B, step)

        @block.tensor
        def _(pe):
            pe.wait_ge(weights_in, 6 * DMA)
            pe.wait_ge(consts_made, 3)
            for src, bank in ((W_in, 0), (Wv_in, 1)):
                for r in range(CT):
                    for c in range(CT):
                        pe.transpose(ps_A[:, bank, c * C + r * P:c * C + (r + 1) * P],
                                     src[:, r, c * P:(c + 1) * P], ident[:])
            pe.matmul(ps_C[:, 1, 0:1], ones[0:1, :], beta_row, start=True, stop=True).then_inc(turned, 1)
            pe.wait_ge(a_spread, 2 * CT)
            pe.wait_ge(turned_copied, 1)
            for t in range(CT):
                pe.matmul(ps_B[:, 0, 0:C], a_rep[:, t, :], WT[:, t, :], start=t == 0, stop=t == CT - 1)
            for c in range(CT):
                for t in range(CT):
                    pe.matmul(ps_B[:, 1, c * P:(c + 1) * P], WT[:, t, c * P:(c + 1) * P], a_rep[:, CT + t, :],
                              start=t == 0, stop=t == CT - 1)
            for c in range(CT):
                for t in range(CT):
                    mm = pe.matmul(ps_C[:, 0, c * C:(c + 1) * C], Wq_in[:, t, c * P:(c + 1) * P], Wk_in[:, t, :],
                                   start=t == 0, stop=t == CT - 1)
            mm.then_inc(made, 1)
            pe.wait_ge(setup_done, 1)

            def products(dsts, lhs, rhs, done=None, before_lo=None):
                n = len(rhs)
                for dst, left in zip(dsts, lhs):
                    for k in range(n):
                        pe.matmul(dst, left[k][0], rhs[k][0], start=k == 0, stop=False)
                if before_lo:
                    before_lo()
                for i, (dst, left) in enumerate(zip(dsts, lhs)):
                    for k in range(n):
                        pe.matmul(dst, left[k][0], rhs[k][1], start=False, stop=False)
                        mm = pe.matmul(dst, left[k][1], rhs[k][0], start=False, stop=k == n - 1)
                    if done:
                        mm.then_inc(done[i], 1)
                return mm

            def product(dst, lhs, rhs):
                return products([dst], [lhs], rhs)

            def turn(src, tile_done, pair_of_banks, done, b):
                for t in range(NT):
                    wait(pe, tile_done[t], b.now)
                    for c in range(CT):
                        tr = pe.transpose(pair_of_banks[:, c, t * P:(t + 1) * P], src[:, t, c * P:(c + 1) * P],
                                          ident[:])
                        if t == NT - 1:
                            tr.then_inc(done[c], 1)

            def both(hi, lo, *where):
                return hi[(slice(None), *where)], lo[(slice(None), *where)]

            def cols(t):
                return slice(t * P, (t + 1) * P)

            def turn_h0(b):
                turn(h0, [h0_done] * NT, ps_B, h0_turned, b)

            def turn_g(b):
                turn(g, [g_done[t // 2] for t in range(NT)], ps_D, g_turned, b)

            def lo_parts(done, b):
                def wait_for_lo():
                    for s in done:
                        wait(pe, s, b.now)
                return wait_for_lo

            def scores2(b):
                for c in range(CT):
                    wait(pe, h0T_lo_done[c], b.now)
                wait(pe, rel_done[2], b.before_rel)
                product(s2_ps, [both(wa2_hi, wa2_lo, c) for c in range(CT)],
                        [both(h0T_hi, h0T_lo, c) for c in range(CT)]).then_inc(s2_done, 1)

            def turn_att(b):
                for t in range(NT):
                    if t == 2:
                        for r in range(2):
                            wait(pe, rel_done[r], b.before)
                    wait(pe, att_done[t], b.now)
                    for j in range(NT):
                        tr = pe.transpose(attT_ps[t][:, cols(j)], att[:, t, cols(j)], ident[:])
                    tr.then_inc(att_turned[t], 1)

            def mix(b):
                wait(pe, h0_lo_done, b.now)
                for t in range(NT):
                    wait(pe, attT_hi_done[t], b.now)
                products([ps_C[:, c, :] for c in range(CT)],
                         [[both(h0_hi, h0_lo, j, cols(c)) for j in range(NT)] for c in range(CT)],
                         [both(attT_hi, attT_lo, j) for j in range(NT)], mix_done, lo_parts([attT_lo_done], b))

            def y_product(b):
                for c in range(CT):
                    wait(pe, mixT_lo_done[c], b.now)
                for t in range(NT):
                    mm = product(rows(ps_A, t), [both(mixT_hi, mixT_lo, k, cols(t)) for k in range(CT)],
                                 [both(W_hi, W_lo, k) for k in range(CT)])
                    if t % 2:
                        mm.then_inc(y_done[t // 2], 1)

            def t_product(b):
                for c in range(CT):
                    wait(pe, gT_hi_done[c], b.now)
                wait(pe, norm_copied, b.before)
                products([ps_C[:, c, :] for c in range(CT)],
                         [[both(G_hi, G_lo, k, cols(c)) for k in range(CT)] for c in range(CT)],
                         [both(gT_hi, gT_lo, k) for k in range(CT)], t_done, lo_parts(gT_lo_done, b))

            def rel_product(b, later):
                for k in range(CT):
                    wait(pe, tT_hi_done[k], b.now)
                    for r in range(2):
                        pe.matmul(rel_ps[r], gT_hi[:, k, cols(r)], tT_hi[:, k], start=k == 0, stop=False)
                        pe.matmul(rel_ps[r], gT_lo[:, k, cols(r)], tT_hi[:, k], start=False, stop=False)
                for k in range(CT):
                    wait(pe, tT_lo_done[k], b.now)
                for r in range(2):
                    for k in range(CT):
                        mm = pe.matmul(rel_ps[r], gT_hi[:, k, cols(r)], tT_lo[:, k], start=False, stop=k == CT - 1)
                    mm.then_inc(rel_mm_done[r], 1)
                if later:
                    for c in range(CT):
                        wait(pe, h0T_lo_done[c], later.now)
                else:
                    wait(pe, out_added[1], b.before)
                products(rel_ps[2:4], [[both(gT_hi, gT_lo, k, cols(r)) for k in range(CT)] for r in (2, 3)],
                         [both(tT_hi, tT_lo, k) for k in range(CT)], rel_mm_done[2:4])

            def aggregate(b, c):
                if c == 0:
                    wait(pe, g_lo_done, b.now)
                    for t in range(NT):
                        wait(pe, rel_lo_done[t], b.now)
                product(ps_D[:, c, :], [both(g_hi, g_lo, j, cols(c)) for j in range(NT)],
                        [both(rel_hi, rel_lo, j) for j in range(NT)]).then_inc(agg_done[c], 1)

            def norms(b):
                wait(pe, sum_sq_done[NT - 2], b.now)
                for t in range(NT):
                    mm = pe.matmul(norm_ps[:, t:t + 1], sum_sq[:, cols(t)], ones[:, 0:1], start=True, stop=True)
                mm.then_inc(norm_mm_done, 1)

            def out_product(b):
                tiles = (0, 2)
                for k in range(CT):
                    wait(pe, aggT_hi_done[k], b.now)
                    for t in tiles:
                        pe.matmul(rows(ps_B, t), aggT_hi[:, k, cols(t)], WvT_hi[:, k], start=k == 0, stop=False)
                        pe.matmul(rows(ps_B, t), aggT_hi[:, k, cols(t)], WvT_lo[:, k], start=False, stop=False)
                    wait(pe, aggT_lo_done[k], b.now)
                    for t in tiles:
                        pe.matmul(rows(ps_B, t), aggT_lo[:, k, cols(t)], WvT_hi[:, k], start=False, stop=k == CT - 1)
                for t in (1, 3):
                    product(rows(ps_B, t), [both(aggT_hi, aggT_lo, k, cols(t)) for k in range(CT)],
                            [both(WvT_hi, WvT_lo, k) for k in range(CT)]).then_inc(out_done[t // 2], 1)

            def step(last, cur, nxt, later):
                if cur:
                    turn_att(cur)
                if nxt:
                    nxt.before_rel = last.now if last else 0
                    scores2(nxt)
                if cur:
                    mix(cur)
                if last:
                    if not nxt:
                        wait(pe, rel_done[NT - 1], last.now)
                    aggregate(last, 0)
                if cur:
                    y_product(cur)
                if last:
                    aggregate(last, 1)
                    norms(last)
                    wait(pe, z_done[NT - 1], nxt.now if nxt else B)
                    wait(pe, rel_done[NT - 1], last.now)
                    out_product(last)
                if cur:
                    turn_g(cur)
                if later:
                    wait(pe, z_done[NT - 1], nxt.now)
                    if last:
                        wait(pe, out_added[1], last.now)
                    turn_h0(later)
                if cur:
                    t_product(cur)
                    rel_product(cur, later)

            first = graph(0)
            first.before_rel = 0
            turn_h0(first)
            scores2(first)
            pe.wait_ge(z_done[NT - 1], 1)
            turn_h0(graph(1))
            run_steps(pe, B, step)


_INS = ["x", "adj", "L0_gnn_W", "L0_gnn_a", "L0_gnn_beta", "L1_gnn_Wq", "L1_gnn_Wk", "L1_gnn_Wv"]


def kernel(**inputs):
    import numpy as np
    import concourse.bacc as bacc
    from concourse.bass_utils import run_bass_kernel_spmd

    nc = bacc.Bacc("TRN2", target_bir_lowering=False, num_devices=1)
    arrays, args = {}, []
    for name in _INS:
        v = np.ascontiguousarray(inputs[name])
        arrays[f"in_{name}"] = v
        args.append(nc.dram_tensor(f"in_{name}", v.shape, mybir.dt.from_np(v.dtype), kind="ExternalInput").ap())
    out = nc.dram_tensor("out", inputs["x"].shape, F32, kind="ExternalOutput").ap()
    build(nc, *args, out)
    result = run_bass_kernel_spmd(nc, [arrays], core_ids=[0])
    return result.results[0]["out"]
```
